# Optimizing a Trainium2 kernel written in Bass

```python
import numpy as np
import jax
import jax.numpy as jnp

def _softmax(x, axis=-1):
    return jax.nn.softmax(x, axis=axis)

def _gelu(x):
    return jax.nn.gelu(x, approximate=True)

def _silu(x):
    return jax.nn.silu(x)

def _sigmoid(x):
    return jax.nn.sigmoid(x)

def _layernorm(x, axis=-1, eps=1e-05):
    m = jnp.mean(x, axis=axis, keepdims=True)
    v = jnp.var(x, axis=axis, keepdims=True)
    return (x - m) / jnp.sqrt(v + eps)

def _scatter_add(tgt, idx, src, axis=0):
    return tgt.at[idx].add(src)

def _segment_sum(src, seg, n):
    return jax.ops.segment_sum(src, seg, n)
kernel_name = 'mk_adj_preln_d2_adj_r2_7c07cb'

def setup_inputs(seed: int=0):
    np.random.seed(seed)
    _w = jnp.asarray

    def _rec_inputs():
        import jax
        import jax.numpy as jnp
        _gk = jax.random.key(seed)
        x = -0.0002928 + 1 * jax.random.normal(jax.random.fold_in(_gk, 1), (128, 128, 256), jnp.float32)
        _a = jax.random.bernoulli(jax.random.fold_in(_gk, 2), 0.0625, (128, 128, 128))
        adj = _a.astype(jnp.int32)
        return (x, adj)
    x, adj = _rec_inputs()

    def _L0_gnn_setup():
        import jax, jax.numpy as jnp
        import numpy as np
        L = 3
        D = 256
        B, N = (8, 512)
        EPS = 1e-05

        def layernorm(x, gamma, beta):
            mu = jnp.mean(x, axis=-1, keepdims=True)
            var = jnp.var(x, axis=-1, keepdims=True)
            return (x - mu) * jax.lax.rsqrt(var + EPS) * gamma + beta
        key = jax.random.key(seed)
        ks = jax.random.split(key, 12)
        s = 1.0 / np.sqrt(D)
        node_features = jax.random.normal(ks[0], (B, N, D), dtype=jnp.float32)
        adjacency_matrix = jax.random.randint(ks[1], (B, N, N), 0, 2, dtype=jnp.int32)
        return {'node_features': node_features, 'adjacency_matrix': adjacency_matrix, 'attn_w': jax.random.normal(ks[2], (L, 2 * D), dtype=jnp.float32) * (1.0 / np.sqrt(2 * D)), 'attn_b': jax.random.normal(ks[3], (L,), dtype=jnp.float32) * 0.01, 'W1': jax.random.normal(ks[4], (L, D, 4 * D), dtype=jnp.float32) * s, 'b1': jnp.zeros((L, 4 * D), dtype=jnp.float32), 'W2': jax.random.normal(ks[5], (L, 4 * D, D), dtype=jnp.float32) * (1.0 / np.sqrt(4 * D)), 'b2': jnp.zeros((L, D), dtype=jnp.float32), 'g1': jnp.ones((L, D), dtype=jnp.float32), 'beta1': jnp.zeros((L, D), dtype=jnp.float32), 'g2': jnp.ones((L, D), dtype=jnp.float32), 'beta2': jnp.zeros((L, D), dtype=jnp.float32)}
    _L0_gnn_all = _L0_gnn_setup()
    _L0_gnn_in = {k: v for k, v in _L0_gnn_all.items() if k in ('attn_w', 'attn_b', 'W1', 'b1', 'W2', 'b2', 'g1', 'beta1', 'g2', 'beta2')}
    del _L0_gnn_all

    def _L1_gnn_setup():
        import jax, jax.numpy as jnp
        import numpy as np
        ALPHA = 0.2
        NEG_INF = -1000000000.0
        key = jax.random.key(seed)
        k1, k2, k3, k4, k5 = jax.random.split(key, 5)
        B, N, F_IN, F_OUT = (16, 512, 256, 256)
        graph_input = jax.random.normal(k1, (B, N, F_IN), dtype=jnp.float32)
        adj = jax.random.randint(k2, (B, N, N), 0, 2, dtype=jnp.int32)
        W = jax.random.normal(k3, (F_OUT, F_IN), dtype=jnp.float32) * (1.414 / np.sqrt(F_IN))
        a1 = jax.random.normal(k4, (F_OUT, 1), dtype=jnp.float32) * 0.1
        a2 = jax.random.normal(k5, (F_OUT, 1), dtype=jnp.float32) * 0.1
        return {'graph_input': graph_input, 'adj': adj, 'W': W, 'a1': a1, 'a2': a2}
    _L1_gnn_all = _L1_gnn_setup()
    _L1_gnn_in = {k: v for k, v in _L1_gnn_all.items() if k in ('W', 'a1', 'a2')}
    del _L1_gnn_all
    return {'x': x, 'adj': adj, 'L0_gnn_attn_w': _L0_gnn_in['attn_w'], 'L0_gnn_attn_b': _L0_gnn_in['attn_b'], 'L0_gnn_W1': _L0_gnn_in['W1'], 'L0_gnn_b1': _L0_gnn_in['b1'], 'L0_gnn_W2': _L0_gnn_in['W2'], 'L0_gnn_b2': _L0_gnn_in['b2'], 'L0_gnn_g1': _L0_gnn_in['g1'], 'L0_gnn_beta1': _L0_gnn_in['beta1'], 'L0_gnn_g2': _L0_gnn_in['g2'], 'L0_gnn_beta2': _L0_gnn_in['beta2'], 'L1_gnn_W': _L1_gnn_in['W'], 'L1_gnn_a1': _L1_gnn_in['a1'], 'L1_gnn_a2': _L1_gnn_in['a2']}

def reference(x, adj, L0_gnn_attn_w, L0_gnn_attn_b, L0_gnn_W1, L0_gnn_b1, L0_gnn_W2, L0_gnn_b2, L0_gnn_g1, L0_gnn_beta1, L0_gnn_g2, L0_gnn_beta2, L1_gnn_W, L1_gnn_a1, L1_gnn_a2):
    import jax
    import jax.numpy as jnp

    def _L0_gnn_ref(node_features, adjacency_matrix, attn_w, attn_b, W1, b1, W2, b2, g1, beta1, g2, beta2):
        import jax, jax.numpy as jnp
        import numpy as np
        L = 3
        D = 256
        B, N = (8, 512)
        EPS = 1e-05

        def layernorm(x, gamma, beta):
            mu = jnp.mean(x, axis=-1, keepdims=True)
            var = jnp.var(x, axis=-1, keepdims=True)
            return (x - mu) * jax.lax.rsqrt(var + EPS) * gamma + beta
        n = adjacency_matrix.shape[-1]
        mask = adjacency_matrix.astype(jnp.float32) + jnp.eye(n, dtype=jnp.float32) > 0
        x = node_features
        d = x.shape[-1]
        for l in range(attn_w.shape[0]):
            si = x @ attn_w[l, :d]
            sj = x @ attn_w[l, d:]
            scores = si[:, :, None] + sj[:, None, :] + attn_b[l]
            scores = jnp.where(scores >= 0, scores, 0.2 * scores)
            scores = jnp.where(mask, scores, -jnp.inf)
            attn = jax.nn.softmax(scores, axis=-1)
            agg = jnp.einsum('bij,bjd->bid', attn, x)
            h = layernorm(x + agg, g1[l], beta1[l])
            ff = jax.nn.gelu(h @ W1[l] + b1[l], approximate=False) @ W2[l] + b2[l]
            x = layernorm(h + ff, g2[l], beta2[l])
        return x

    def _L1_gnn_ref(graph_input, adj, W, a1, a2):
        import jax, jax.numpy as jnp
        import numpy as np
        ALPHA = 0.2
        NEG_INF = -1000000000.0
        h = jnp.einsum('bnf,of->bno', graph_input, W)
        f1 = h @ a1
        f2 = h @ a2
        e = f1 + jnp.swapaxes(f2, 1, 2)
        e = jax.nn.leaky_relu(e, negative_slope=ALPHA)
        scores = jnp.where(adj == 0, NEG_INF, e)
        attn = jax.nn.softmax(scores, axis=2)
        h_prime = jnp.einsum('bnm,bmf->bnf', attn, graph_input)
        return jax.nn.elu(h_prime)
    h = jnp.maximum(_layernorm(x, axis=-1), 0.0)
    x = x + _L0_gnn_ref(h, adj, L0_gnn_attn_w, L0_gnn_attn_b, L0_gnn_W1, L0_gnn_b1, L0_gnn_W2, L0_gnn_b2, L0_gnn_g1, L0_gnn_beta1, L0_gnn_g2, L0_gnn_beta2)
    h = jnp.maximum(_layernorm(x, axis=-1), 0.0)
    x = x + _L1_gnn_ref(h, adj, L1_gnn_W, L1_gnn_a1, L1_gnn_a2)
    return x

_drawn_inputs = setup_inputs


def setup_inputs(seed=0):
    import zlib

    import numpy as np

    out = dict(_drawn_inputs(seed))
    spreads = {'L0_gnn_b1': (0.0, 0.1),
     'L0_gnn_b2': (0.0, 0.1),
     'L0_gnn_g1': (1.0, 0.2),
     'L0_gnn_beta1': (0.0, 0.1),
     'L0_gnn_g2': (1.0, 0.2),
     'L0_gnn_beta2': (0.0, 0.1)}
    factors = {'L0_gnn_attn_b': 64.0}
    for name, (base, spread) in spreads.items():
        noise = np.random.default_rng([zlib.crc32(name.encode()), seed]).standard_normal(out[name].shape)
        drawn = base * np.exp(spread * noise) if base else spread * noise
        out[name] = jnp.asarray(drawn.astype(out[name].dtype))
    for name, factor in factors.items():
        out[name] = (out[name] * factor).astype(out[name].dtype)
    return out
```

```python
from contextlib import ExitStack

import concourse.bass as bass
from concourse import mybir

ALU = mybir.AluOpType
ACT = mybir.ActivationFunctionType
AX_X = mybir.AxisListType.X
F32 = mybir.dt.float32
F16 = mybir.dt.float16
BF16 = mybir.dt.bfloat16
I32 = mybir.dt.int32

P = 128
EPS = 1e-5
SLOPE = 0.2
BIG = float(2.0 ** 100)
WSCALE = 64.0
LEAST = -3.0e38

GB = 4
SLOTS = 4
FIRST = -3


def graph_networks_kernel(nc, x, adj, attn_w, attn_b, W1, b1, W2, b2, g1, beta1, g2, beta2,
                          L1_W, L1_a1, L1_a2, out):
    B, NODES, D = x.shape
    L = attn_w.shape[0]
    F = W1.shape[2]
    assert NODES == P and D == 2 * P and F % P == 0 and B % (GB * SLOTS) == 0
    KD = D // P
    MF = F // P
    T = GB * P
    PER = L * SLOTS
    ITERS = B // (GB * SLOTS)
    STAGES = ITERS * PER
    GROUPS = ITERS * SLOTS
    LAG1 = PER - 2
    assert L == 3 and ITERS >= 3
    LAST = 3 * (GROUPS - 1) + LAG1 + 2

    def stage(it, k, per, upto):
        return it * (PER * per) + (k * per + upto)

    def group(it, s, per, upto):
        return it * (SLOTS * per) + (s * per + upto)

    def has(it, k):
        return not isinstance(it, int) or 0 <= it * PER + k < STAGES

    def has_group(it, s):
        return not isinstance(it, int) or 0 <= it * SLOTS + s < GROUPS

    def layer(k):
        return (k % PER) // SLOTS

    def l1_of(k):
        return (k - LAG1) // 3, (k - LAG1) % 3

    def apart(eng):
        eng.sem_inc(carrier, 1)

    def walk(eng, window):
        for k in range(FIRST, PER):
            window(0, k)
        with eng.Fori(1, ITERS - 1) as it:
            for k in range(PER):
                window(it, k)
        for k in range(LAST + 1 - (ITERS - 1) * PER):
            window(ITERS - 1, k)

    with ExitStack() as ctx:
        def sb(name, shape, dt=F32):
            return ctx.enter_context(nc.sbuf_tensor(name, [P] + shape, dt))

        def bank(name):
            return ctx.enter_context(nc.psum_tensor(name, [P, T], F32))

        def sem(name):
            return ctx.enter_context(nc.semaphore(name))

        psH = [bank(f"psH{i}") for i in range(2)]
        psY = [bank(f"psY{i}") for i in range(2)]
        psG = [bank(f"psG{i}") for i in range(2)]
        psT0 = bank("psT0")
        psT1 = bank("psT1")

        w1h = sb("w1h", [L, KD, F], F16)
        w1l = sb("w1l", [L, KD, F], F16)
        w2h = sb("w2h", [L, MF, D], F16)
        w2l = sb("w2l", [L, MF, D], F16)
        b1col = sb("b1col", [L, MF])
        b1raw = sb("b1raw", [L, MF])
        g1col = sb("g1col", [L, KD])
        g1s = sb("g1s", [L, KD])
        be1col = sb("be1col", [L, KD])
        rows = sb("rows", [L, 6, D])
        abias = sb("abias", [L, 1])
        l1w = sb("l1w", [KD, D])
        l1a = sb("l1a", [KD, 2])
        uu = sb("uu", [2, D])
        ident = sb("ident", [P])
        onescol = sb("onescol", [2])
        mhalf = sb("mhalf", [GB])

        xin = sb("xin", [GB, D])
        adjin = sb("adjin", [GB, P], I32)
        adjt = sb("adjt", [GB, P])
        xs = [sb(f"xs{i}", [GB, D]) for i in range(SLOTS)]
        x1 = [sb(f"x1_{i}", [GB, D]) for i in range(SLOTS)]
        mask0 = [sb(f"mask0_{i}", [GB, P], BF16) for i in range(SLOTS)]
        scol = [sb(f"scol{i}", [2 * GB]) for i in range(SLOTS)]
        junk = sb("junk", [2 * GB, D], BF16)

        vv = sb("vv", [GB, P])
        e1 = sb("e1", [GB, P])
        e2 = sb("e2", [GB, P])
        pts = sb("pts", [GB, P])
        sm = sb("sm", [8, GB])
        rinv = sb("rinv", [GB])
        yb = sb("yb", [GB, D])
        st1 = sb("st1", [GB, 6])
        mv1 = sb("mv1", [GB, 2])
        ln1 = sb("ln1", [4, GB])
        rb = [sb(f"rb{i}", [GB, D]) for i in range(2)]
        hth = [sb(f"hth{i}", [KD, T], F16) for i in range(2)]
        htl = [sb(f"htl{i}", [KD, T], F16) for i in range(2)]

        gf = [sb(f"gf{i}", [T]) for i in range(3)]
        ghi = sb("ghi", [MF, T], F16)
        glo = sb("glo", [MF, T], F16)
        rr = sb("rr", [GB, D])
        st2 = sb("st2", [GB, 6])
        mv2 = sb("mv2", [GB, 2])
        ln2 = sb("ln2", [4, GB])

        st0 = sb("st0", [GB, 6])
        mv0 = sb("mv0", [GB, 2])
        ln0 = sb("ln0", [4, GB])

        adj1 = sb("adj1", [GB, P], I32)
        mask1 = sb("mask1", [GB, P], BF16)
        st3 = sb("st3", [GB, 6])
        mv3 = sb("mv3", [GB, 2])
        ln3 = sb("ln3", [4, GB])
        hl = sb("hl", [GB, D])
        lscol = sb("lscol", [2 * GB])
        lv = sb("lv", [GB, P])
        le1 = sb("le1", [GB, P])
        le2 = sb("le2", [GB, P])
        lpts = sb("lpts", [GB, P])
        lsm = sb("lsm", [8, GB])
        lrinv = sb("lrinv", [GB])
        hp = sb("hp", [GB, D])
        ea = sb("ea", [GB, D])
        b2row = ea[:, 0:L, :]
        ob = [sb(f"ob{i}", [GB, D]) for i in range(2)]

        stage_w = [g[:].rearrange("p a b -> p (a b)").bitcast(F32) for g in (ghi, glo)]

        consts_in = sem("consts_in")
        stage_in = [sem(f"stage_in{i}") for i in range(2)]
        x_in = sem("x_in")
        adj_in = sem("adj_in")
        res_in = [sem(f"res_in{i}") for i in range(SLOTS)]
        adj1_in = sem("adj1_in")
        out_st = [sem(f"out_st{i}") for i in range(2)]

        made = sem("made")
        zeroed = sem("zeroed")
        carrier = sem("carrier")
        b1_ps = sem("b1_ps")
        b1_ok = sem("b1_ok")
        uu_ps = sem("uu_ps")
        uu_ok = sem("uu_ok")
        scaled = sem("scaled")
        w_hi = sem("w_hi")
        w_ok = sem("w_ok")

        p_stats = sem("p_stats")
        p_small = sem("p_small")
        relu_ok = sem("relu_ok")
        mask0_ok = sem("mask0_ok")
        score_cols = sem("score_cols")
        sj_ps = sem("sj_ps")
        masked = sem("masked")
        soft_small = sem("soft_small")
        exps = sem("exps")
        probs = sem("probs")
        pt_ps = sem("pt_ps")
        pt_ok = sem("pt_ok")
        agg_ps = sem("agg_ps")
        y_ok = sem("y_ok")
        ln1_small = sem("ln1_small")
        n_ok = sem("n_ok")
        nt_ps = sem("nt_ps")
        h_hi = sem("h_hi")
        h_lo = sem("h_lo")
        rb_ok = sem("rb_ok")
        ffn1_ps = sem("ffn1_ps")
        gelu_ok = sem("gelu_ok")
        g_hi = sem("g_hi")
        g_ok = sem("g_ok")
        ffn2_ps = sem("ffn2_ps")
        r_ok = sem("r_ok")
        ln2_stats = sem("ln2_stats")
        ln2_small = sem("ln2_small")
        n2_ok = sem("n2_ok")
        x_ok = sem("x_ok")
        x1_ok = sem("x1_ok")

        l_stats = sem("l_stats")
        l_small = sem("l_small")
        l_relu = sem("l_relu")
        mask1_ok = sem("mask1_ok")
        l_cols = sem("l_cols")
        l_sj = sem("l_sj")
        l_masked = sem("l_masked")
        l_soft = sem("l_soft")
        l_exps = sem("l_exps")
        l_probs = sem("l_probs")
        l_pt = sem("l_pt")
        l_pt_ok = sem("l_pt_ok")
        l_agg = sem("l_agg")
        l_hp = sem("l_hp")
        l_min = sem("l_min")
        l_ea = sem("l_ea")
        l_out = sem("l_out")

        x_dram = x.rearrange("(g b) n d -> n g b d", b=GB)
        out_dram = out.rearrange("(g b) n d -> n g b d", b=GB)
        adj_dram = adj.rearrange("(g b) i j -> i g b j", b=GB)
        CONSTS = 10 * L + 3

        def grp(dram, it, s):
            return dram[:, bass.ds(it * SLOTS + s, 1), :, :].rearrange("n g b d -> n (g b) d")

        def flat(t):
            return t.rearrange("p b d -> p (b d)")

        block = ctx.enter_context(nc.Block())

        @block.sync
        def _(sp):
            def piece(n):
                if n >= 2:
                    sp.wait_ge(w_ok, n - 1)
                src = (W1 if n % 2 == 0 else W2)[n // 2].rearrange("(k p) f -> p k f", p=P)
                dst = stage_w[n % 2].rearrange("p (k f) -> p k f", k=src.shape[1])
                sp.dma_start(dst, src).then_inc(stage_in[n % 2], 16)

            def load_group(it, s):
                if not isinstance(it, int) or it * SLOTS + s >= 1:
                    sp.wait_ge(relu_ok, group(it, s, 1, 0))
                    apart(sp)
                    sp.wait_ge(mask0_ok, group(it, s, 3, 0))
                apart(sp)
                sp.dma_start(xin[:], grp(x_dram, it, s)).then_inc(x_in, 16)
                sp.dma_start(adjin[:], grp(adj_dram, it, s)).then_inc(adj_in, 16)

            load_group(0, 0)
            for l in range(L):
                for src, dst in ((b1, b1raw), (g1, g1col), (beta1, be1col)):
                    with nc.allow_non_contiguous_dma(reason="a small constant"):
                        sp.dma_start(dst[:, l, :], src[l].rearrange("(k p) -> p k", p=P)).then_inc(consts_in, 16)
                for dst, src in ((rows[:, l, 0], g1[l:l + 1]), (rows[:, l, 1], beta1[l:l + 1]),
                                 (rows[:, l, 2], g2[l:l + 1]), (rows[:, l, 3], beta2[l:l + 1]),
                                 (b2row[:, l, :], b2[l:l + 1]),
                                 (rows[:, l, 4:6], attn_w[l:l + 1])):
                    dst = dst if len(dst.shape) == 2 else dst.rearrange("p a d -> p (a d)")
                    sp.dma_start(dst, src.broadcast_to((P, src.shape[1]))).then_inc(consts_in, 16)
                with nc.allow_non_contiguous_dma(reason="a small constant"):
                    sp.dma_start(abias[:, l], attn_b[l:l + 1].rearrange("(a b) -> a b", a=1).broadcast_to((P, 1))).then_inc(consts_in, 16)
            sp.dma_start(l1w[:], L1_W.rearrange("(k p) f -> p k f", p=P)).then_inc(consts_in, 16)
            with nc.allow_non_contiguous_dma(reason="a small constant"):
                for i, a in enumerate((L1_a1, L1_a2)):
                    sp.dma_start(l1a[:, :, i:i + 1], a.rearrange("(k p) o -> p k o", p=P)).then_inc(consts_in, 16)
            piece(0)
            piece(1)

            def window(it, k):
                if has(it, k + 4) and layer(k + 4) == 0:
                    load_group(it, (k + 4) // PER * SLOTS + (k + 4) % PER)
                if isinstance(it, int) and it == 0 and FIRST <= k < FIRST + L - 1:
                    piece(2 * (k - FIRST) + 2)
                    piece(2 * (k - FIRST) + 3)
                if has(it, k) and layer(k) == 2:
                    s = k % SLOTS
                    if not isinstance(it, int) or it >= 1:
                        sp.wait_ge(l_out, group(it, s - SLOTS, 2, 2))
                    apart(sp)
                    sp.dma_start(x1[s][:], grp(x_dram, it, s)).then_inc(res_in[s], 16)
                q, phase = l1_of(k)
                if has_group(it, q):
                    if phase == 0:
                        if not isinstance(it, int) or it * SLOTS + q >= 1:
                            sp.wait_ge(mask1_ok, group(it, q, 1, 0))
                        apart(sp)
                        sp.dma_start(adj1[:], grp(adj_dram, it, q)).then_inc(adj1_in, 16)
                    if phase == 2:
                        sp.wait_ge(l_out, group(it, q, 2, 2))
                        apart(sp)
                        sp.dma_start(grp(out_dram, it, q), ob[q % 2][:]).then_inc(out_st[q % 2], 16)

            walk(sp, window)
            for o in out_st:
                sp.wait_ge(o, 16 * (GROUPS // 2))

        @block.tensor
        def _(pe):
            def hidden_bias(l):
                pe.wait_ge(stage_in[0], 16 * (l + 1))
                if l == 0:
                    pe.wait_ge(consts_in, 16 * CONSTS)
                w = stage_w[0].rearrange("p (k f) -> p k f", k=KD)
                if l >= 1:
                    pe.wait_ge(b1_ok, l)
                for m in range(MF):
                    for c in range(KD):
                        last = pe.matmul(psH[0][:, m:m + 1], w[:, c, m * P:(m + 1) * P],
                                         be1col[:, l, c:c + 1], start=(c == 0), stop=(c == KD - 1))
                last.then_inc(b1_ps, 1)

            def folded_scores():
                for i in range(2):
                    for c in range(KD):
                        last = pe.matmul(psH[1][:, i * D:(i + 1) * D],
                                         l1a[:, c, i:i + 1].broadcast_to((P, P)), l1w[:, c, :],
                                         start=(c == 0), stop=(c == KD - 1))
                last.then_inc(uu_ps, 1)

            def score_rows(cols, done):
                for b in range(GB):
                    last = pe.matmul(psT0[:, b * P:(b + 1) * P], cols[:, b:b + 1].broadcast_to((P, P)),
                                     ident[:], start=True, stop=True)
                last.then_inc(done, 1)

            def turn_probs(src, done):
                for b in range(GB):
                    last = pe.transpose(psT1[:, b * P:(b + 1) * P], src[:, b, :], ident[:])
                last.then_inc(done, 1)

            def aggregate(pt, vals, done):
                for b in range(GB):
                    last = pe.matmul(psT0[:, b:b + 1], pt[:, b, :], onescol[:, 0:1], start=True, stop=True)
                last.then_inc(done, 1)
                for b in range(GB):
                    last = pe.matmul(psG[b // 2][:, b % 2 * D:(b % 2 + 1) * D], pt[:, b, :], vals[:, b, :],
                                     start=True, stop=True)
                    if b % 2:
                        last.then_inc(done, 1)

            def ffn1(it, k, m):
                l, h = layer(k), k % 2
                if m == 0:
                    pe.wait_ge(h_lo, stage(it, k, 2, 2))
                    if isinstance(it, int) and it == 0 and k % SLOTS == 0:
                        pe.wait_ge(w_ok, 2 * l + 2)
                if m >= 2:
                    pe.wait_ge(gelu_ok, stage(it, k, MF, m - 1))
                n = 0
                for c in range(KD):
                    for w, t in ((w1h, hth), (w1h, htl), (w1l, hth)):
                        last = pe.matmul(psH[m % 2][:], w[:, l, c, m * P:(m + 1) * P], t[h][:, c, :],
                                         start=(n == 0), stop=(n == 3 * KD - 1))
                        n += 1
                last.then_inc(ffn1_ps, 1)

            def ffn2(it, k, b):
                l = layer(k)
                if b % 2 == 0 and has(it, k - 1):
                    pe.wait_ge(r_ok, stage(it, k - 1, 2, b // 2 + 1))
                for c in range(MF):
                    if b == 0:
                        pe.wait_ge(g_ok, stage(it, k, MF, c + 1))
                    for n, (g, w) in enumerate(((ghi, w2h), (ghi, w2l), (glo, w2h))):
                        last = pe.matmul(psY[b // 2][:, b % 2 * D:(b % 2 + 1) * D],
                                         g[:, c, b * P:(b + 1) * P], w[:, l, c, :],
                                         start=(c == 0 and n == 0), stop=(c == MF - 1 and n == 2))
                if b % 2:
                    last.then_inc(ffn2_ps, 1)

            pe.wait_ge(made, 2)
            hidden_bias(0)
            folded_scores()

            def window(it, k):
                q, phase = l1_of(k)
                l1 = has_group(it, q)
                if isinstance(it, int) and it == 0 and FIRST < k < FIRST + L:
                    hidden_bias(k - FIRST)
                for step in range(MF + GB):
                    if step == 0 and has(it, k + 1):
                        pe.wait_ge(probs, stage(it, k + 1, 1, 1))
                        turn_probs(e1, pt_ps)
                    if has(it, k):
                        if step < MF:
                            ffn1(it, k, step)
                        else:
                            ffn2(it, k, step - MF)
                    if step == 1 and has(it, k + 1):
                        pe.wait_ge(pt_ok, stage(it, k + 1, 1, 1))
                        if k % 3 == (LAG1 + 3) % 3 and has_group(it, l1_of(k - 1)[0]):
                            pe.wait_ge(l_hp, group(it, l1_of(k - 1)[0], 3, 3))
                        aggregate(pts, xs[(k + 1) % SLOTS], agg_ps)
                    if step == 3 and l1 and phase == 2:
                        pe.wait_ge(l_probs, group(it, q, 1, 1))
                        turn_probs(le1, l_pt)
                    if step == 4 and l1 and phase == 1:
                        if has(it, k + 1):
                            pe.wait_ge(y_ok, stage(it, k + 1, 5, 1))
                        pe.wait_ge(l_cols, group(it, q, 1, 1))
                        score_rows(lscol, l_sj)
                    if step == 4 and l1 and phase == 2:
                        if has(it, k + 1):
                            pe.wait_ge(y_ok, stage(it, k + 1, 5, 3))
                        pe.wait_ge(l_pt_ok, group(it, q, 1, 1))
                        aggregate(lpts, hl, l_agg)
                    if step == 6 and has(it, k + 1):
                        pe.wait_ge(n_ok, stage(it, k + 1, 1, 1))
                        if l1 and phase == 1:
                            pe.wait_ge(l_masked, group(it, q, 1, 1))
                        if l1 and phase == 2:
                            pe.wait_ge(l_hp, group(it, q, 3, 1))
                        for c, ps in enumerate((psT0, psT1)):
                            for b in range(GB):
                                last = pe.transpose(ps[:, b * P:(b + 1) * P], yb[:, b, c * P:(c + 1) * P], ident[:])
                            last.then_inc(nt_ps, 1)
                    if step == 7 and has(it, k + 2):
                        if has(it, k + 1):
                            pe.wait_ge(h_lo, stage(it, k + 1, 2, 1))
                        elif l1 and phase == 1:
                            pe.wait_ge(l_masked, group(it, q, 1, 1))
                        pe.wait_ge(score_cols, stage(it, k + 2, 1, 1))
                        score_rows(scol[(k + 2) % SLOTS], sj_ps)

            walk(pe, window)

        @block.scalar
        def _(act):
            def scale_piece(n):
                l = n // 2
                act.wait_ge(stage_in[n % 2], 16 * (l + 1))
                if n % 2 == 0:
                    act.wait_ge(b1_ps, l + 1)
                    for c in range(KD):
                        w = stage_w[0][:, c * F:(c + 1) * F]
                        last = act.activation(w, w, ACT.Copy, scale=g1s[:, l, c:c + 1])
                else:
                    last = act.activation(stage_w[1], stage_w[1], ACT.Copy, scale=WSCALE)
                last.then_inc(scaled, 1)

            def norm(dst, src, ln, func):
                for b in range(GB):
                    last = act.activation(dst[:, b, :], src[:, b, :], func,
                                          bias=ln[:, 3, b:b + 1], scale=ln[:, 1, b:b + 1])
                return last

            def two_exps(v, s, ea_, eb_):
                for b in range(GB):
                    act.activation(ea_[:, b, :], v[:, b, :], ACT.Exp, bias=s[:, 4, b:b + 1])
                for b in range(GB):
                    last = act.activation(eb_[:, b, :], v[:, b, :], ACT.Exp, bias=s[:, 6, b:b + 1], scale=SLOPE)
                return last

            def gelu(it, k, m):
                act.wait_ge(ffn1_ps, stage(it, k, MF, m + 1))
                if has(it, k - 1) or m >= 3:
                    act.wait_ge(g_ok, stage(it, k, MF, m - 2))
                n = (k * MF + m) % 3
                act.activation(gf[n][:], psH[m % 2][:], ACT.Gelu, bias=b1col[:, layer(k), m:m + 1],
                               scale=1.0 / WSCALE).then_inc(gelu_ok, 1)

            act.wait_ge(made, 4)
            act.wait_ge(b1_ps, 1)
            scale_piece(0)
            scale_piece(1)

            def window(it, k):
                q, phase = l1_of(k)
                l1 = has_group(it, q)
                if isinstance(it, int) and it == 0 and FIRST < k < FIRST + L:
                    scale_piece(2 * (k - FIRST))
                    scale_piece(2 * (k - FIRST) + 1)
                if isinstance(it, int) and it == 0 and k == 0:
                    act.wait_ge(b1_ok, L)
                for step in range(MF + GB):
                    if step == 0 and has(it, k + 1):
                        act.wait_ge(pt_ps, stage(it, k + 1, 1, 1))
                        act.activation(flat(pts[:]), psT1[:], ACT.Copy).then_inc(pt_ok, 1)
                    if step < MF and has(it, k):
                        gelu(it, k, step)
                    if step == 1 and has(it, k - 1):
                        act.wait_ge(ln2_small, stage(it, k - 1, 4, 4))
                        norm(rr, rr, ln2, ACT.Identity).then_inc(n2_ok, 1)
                    if step == 2 and has(it, k + 3) and layer(k + 3) == 0:
                        g = (k + 3) // PER * SLOTS + (k + 3) % PER
                        act.wait_ge(p_small, group(it, g, 4, 4))
                        norm(xs[g % SLOTS], xin, ln0, ACT.Relu).then_inc(relu_ok, 1)
                    if step == 3 and l1 and phase == 0:
                        act.wait_ge(l_small, group(it, q, 4, 4))
                        norm(hl, x1[q % SLOTS], ln3, ACT.Relu).then_inc(l_relu, 1)
                    if step == 3 and l1 and phase == 2:
                        act.wait_ge(l_pt, group(it, q, 1, 1))
                        act.activation(flat(lpts[:]), psT1[:], ACT.Copy).then_inc(l_pt_ok, 1)
                    if step == 5 and has(it, k + 1):
                        act.wait_ge(ln1_small, stage(it, k + 1, 4, 4))
                        norm(yb, yb, ln1, ACT.Identity).then_inc(n_ok, 1)
                    if step == 6 and has(it, k + 1):
                        for c, ps in enumerate((psT0, psT1)):
                            act.wait_ge(nt_ps, stage(it, k + 1, 2, c + 1))
                            act.activation(hth[(k + 1) % 2][:, c, :], ps[:], ACT.Copy).then_inc(h_hi, 1)
                    if step == MF + 1 and has(it, k + 2):
                        act.wait_ge(soft_small, stage(it, k + 2, 8, 8))
                        two_exps(vv, sm, e1, e2).then_inc(exps, 1)
                    if step == MF + 1 and l1 and phase == 1:
                        act.wait_ge(l_soft, group(it, q, 7, 7))
                        two_exps(lv, lsm, le1, le2).then_inc(l_exps, 1)
                    if step == MF + 1 and l1 and phase == 2:
                        act.wait_ge(l_min, group(it, q, 1, 1))
                        act.activation(ea[:], ea[:], ACT.Exp).then_inc(l_ea, 1)

            walk(act, window)

        @block.vector
        def _(dve):
            def split_piece(n):
                l = n // 2
                hi, lo = ((w1h, w1l), (w2h, w2l))[n % 2]
                hi, lo = (t[:, l].rearrange("p a b -> p (a b)") for t in (hi, lo))
                dve.wait_ge(scaled, n + 1)
                dve.tensor_copy(hi, stage_w[n % 2]).then_inc(w_hi, 1)
                dve.wait_ge(w_hi, n + 1)
                dve.tensor_tensor(lo, stage_w[n % 2], hi, ALU.subtract).then_inc(w_ok, 1)

            def hidden_bias(l):
                dve.wait_ge(b1_ps, l + 1)
                dve.tensor_tensor(b1col[:, l, :], psH[0][:, 0:MF], b1raw[:, l, :], ALU.add).then_inc(b1_ok, 1)

            def stats(src, st, lo, hi):
                for b in range(lo, hi):
                    last = dve.bn_stats(st[:, b, :], src[:, b, :])
                return last

            def mean_var(st, mv):
                apart(dve)
                for b in range(GB):
                    last = dve.bn_aggr(mv[:, b, :], st[:, b, :])
                return last

            def dot_scores(src, wj, wi, cols):
                for h, w in enumerate((wj, wi)):
                    for b in range(GB):
                        last = dve.tensor_tensor_reduce(junk[:, h * GB + b, :], src[:, b, :], w, 1.0, 0.0,
                                                        ALU.mult, ALU.add, cols[:, h * GB + b:h * GB + b + 1])
                return last

            def mask_rows(mask, v, s):
                apart(dve)
                for b in range(GB):
                    last = dve.tensor_tensor_reduce(v[:, b, :], psT0[:, b * P:(b + 1) * P], mask[:, b, :], 1.0,
                                                    LEAST, ALU.add, ALU.max, s[:, 0, b:b + 1])
                return last

            def gelu_parts(it, k, m):
                n = (k * MF + m) % 3
                dve.wait_ge(gelu_ok, stage(it, k, MF, m + 1))
                dve.tensor_copy(ghi[:, m, :], gf[n][:]).then_inc(g_hi, 1)
                dve.wait_ge(g_hi, stage(it, k, MF, m + 1))
                dve.tensor_tensor(glo[:, m, :], gf[n][:], ghi[:, m, :], ALU.subtract).then_inc(g_ok, 1)

            def residual(it, k, pr):
                dve.wait_ge(ffn2_ps, stage(it, k, 2, pr + 1))
                dve.wait_ge(rb_ok, stage(it, k, 2, 2))
                if pr == 0 and has(it, k - 1):
                    dve.wait_ge(x_ok, stage(it, k - 1, 2, 2))
                    if layer(k - 1) == 2:
                        dve.wait_ge(x1_ok, group(it, (k - 1) // PER * SLOTS + (k - 1) % SLOTS, 1, 1))
                dst = flat(rr[:, 2 * pr:2 * pr + 2, :])
                dve.scalar_tensor_tensor(out=dst, in0=psY[pr][:], scalar=1.0 / WSCALE,
                                         in1=flat(rb[k % 2][:, 2 * pr:2 * pr + 2, :]),
                                         op0=ALU.mult, op1=ALU.add).then_inc(r_ok, 1)
                dve.wait_ge(r_ok, stage(it, k, 2, pr + 1))
                stats(rr, st2, 2 * pr, 2 * pr + 2).then_inc(ln2_stats, 1)

            dve.wait_ge(consts_in, 16 * CONSTS)
            hidden_bias(0)
            dve.wait_ge(uu_ps, 1)
            dve.tensor_copy(uu[:].rearrange("p a d -> p (a d)"), psH[1][:]).then_inc(uu_ok, 1)
            split_piece(0)
            split_piece(1)

            def window(it, k):
                q, phase = l1_of(k)
                l1 = has_group(it, q)
                if isinstance(it, int) and it == 0 and FIRST < k < FIRST + L:
                    hidden_bias(k - FIRST)
                    split_piece(2 * (k - FIRST))
                    split_piece(2 * (k - FIRST) + 1)
                for step in range(MF + GB):
                    if step == 0 and has(it, k - 1):
                        residual(it, k - 1, 1)
                        dve.wait_ge(ln2_stats, stage(it, k - 1, 3, 2))
                        mean_var(st2, mv2).then_inc(ln2_stats, 1)
                    if step == 1 and has(it, k + 3) and layer(k + 3) == 0:
                        g = (k + 3) // PER * SLOTS + (k + 3) % PER
                        dve.wait_ge(x_in, group(it, g, 16, 16))
                        stats(xin, st0, 0, GB).then_inc(p_stats, 1)
                        dve.wait_ge(p_stats, group(it, g, 2, 1))
                        mean_var(st0, mv0).then_inc(p_stats, 1)
                    if step == 2 and l1 and phase == 0:
                        dve.wait_ge(x1_ok, group(it, q, 1, 1))
                        stats(x1[q % SLOTS], st3, 0, GB).then_inc(l_stats, 1)
                        dve.wait_ge(l_stats, group(it, q, 2, 1))
                        mean_var(st3, mv3).then_inc(l_stats, 1)
                    if step < MF and has(it, k):
                        gelu_parts(it, k, step)
                    if step == 2 and has(it, k + 1):
                        s = (k + 1) % SLOTS
                        dve.wait_ge(agg_ps, stage(it, k + 1, 3, 1))
                        dve.reciprocal(rinv[:], psT0[:, 0:GB]).then_inc(y_ok, 1)
                        dve.wait_ge(y_ok, stage(it, k + 1, 5, 1))
                        if has(it, k):
                            dve.wait_ge(rb_ok, stage(it, k, 2, 1))
                        for b in range(GB):
                            if b % 2 == 0:
                                dve.wait_ge(agg_ps, stage(it, k + 1, 3, 2 + b // 2))
                            last = dve.scalar_tensor_tensor(
                                out=yb[:, b, :], in0=psG[b // 2][:, b % 2 * D:(b % 2 + 1) * D],
                                scalar=rinv[:, b:b + 1], in1=xs[s][:, b, :], op0=ALU.mult, op1=ALU.add)
                            if b % 2:
                                last.then_inc(y_ok, 1)
                        dve.wait_ge(y_ok, stage(it, k + 1, 5, 3))
                        stats(yb, st1, 0, GB).then_inc(y_ok, 1)
                        dve.wait_ge(y_ok, stage(it, k + 1, 5, 4))
                        mean_var(st1, mv1).then_inc(y_ok, 1)
                    if step == 4 and has(it, k + 3):
                        s = (k + 3) % SLOTS
                        if layer(k + 3) == 0:
                            g = (k + 3) // PER * SLOTS + (k + 3) % PER
                            dve.wait_ge(relu_ok, group(it, g, 1, 1))
                        else:
                            dve.wait_ge(x_ok, stage(it, k - 1, 2, 2))
                        if has(it, k + 2):
                            dve.wait_ge(score_cols, stage(it, k + 2, 1, 1))
                        if has_group(it, l1_of(k)[0] - (phase == 0)) :
                            dve.wait_ge(l_cols, group(it, l1_of(k)[0] - (phase == 0), 1, 1))
                        lay = layer(k + 3)
                        dot_scores(xs[s], rows[:, lay, 5, :], rows[:, lay, 4, :], scol[s]).then_inc(score_cols, 1)
                    if step == 5 and l1 and phase == 0:
                        if has(it, k + 3):
                            dve.wait_ge(score_cols, stage(it, k + 3, 1, 1))
                        elif has_group(it, q - 1):
                            dve.wait_ge(l_cols, group(it, q - 1, 1, 1))
                        dve.wait_ge(l_relu, group(it, q, 1, 1))
                        dot_scores(hl, uu[:, 1, :], uu[:, 0, :], lscol).then_inc(l_cols, 1)
                    if step == 5 and l1 and phase == 1:
                        dve.wait_ge(l_sj, group(it, q, 1, 1))
                        dve.wait_ge(mask1_ok, group(it, q, 1, 1))
                        mask_rows(mask1, lv, lsm).then_inc(l_masked, 1)
                    if step == 5 and l1 and phase == 2:
                        dve.wait_ge(l_agg, group(it, q, 3, 1))
                        dve.reciprocal(lrinv[:], psT0[:, 0:GB]).then_inc(l_hp, 1)
                        dve.wait_ge(l_hp, group(it, q, 3, 1))
                        for b in range(GB):
                            if b % 2 == 0:
                                dve.wait_ge(l_agg, group(it, q, 3, 2 + b // 2))
                            last = dve.tensor_scalar(hp[:, b, :], psG[b // 2][:, b % 2 * D:(b % 2 + 1) * D],
                                                     lrinv[:, b:b + 1], None, ALU.mult)
                            if b % 2:
                                last.then_inc(l_hp, 1)
                    if step == 6 and has(it, k + 1):
                        for c, ps in enumerate((psT0, psT1)):
                            dve.wait_ge(h_hi, stage(it, k + 1, 2, c + 1))
                            dve.tensor_tensor(htl[(k + 1) % 2][:, c, :], ps[:], hth[(k + 1) % 2][:, c, :],
                                              ALU.subtract).then_inc(h_lo, 1)
                    if step == MF and has(it, k + 2):
                        dve.wait_ge(sj_ps, stage(it, k + 2, 1, 1))
                        if layer(k + 2) == 0:
                            g = (k + 2) // PER * SLOTS + (k + 2) % PER
                            dve.wait_ge(mask0_ok, group(it, g, 3, 3))
                        mask_rows(mask0[(k + 2) % SLOTS], vv, sm).then_inc(masked, 1)
                    if step == MF + 1 and l1 and phase == 2:
                        dve.wait_ge(l_hp, group(it, q, 3, 3))
                        if not isinstance(it, int) or it * SLOTS + q >= 2:
                            dve.wait_ge(out_st[q % 2], it * (16 * SLOTS // 2) + 16 * (q // 2))
                        dve.scalar_tensor_tensor(out=flat(ob[q % 2][:]), in0=flat(hp[:]), scalar=0.0,
                                                 in1=flat(x1[q % SLOTS][:]), op0=ALU.max, op1=ALU.add).then_inc(l_out, 1)
                        dve.wait_ge(l_out, group(it, q, 2, 1))
                        dve.wait_ge(l_ea, group(it, q, 1, 1))
                        dve.scalar_tensor_tensor(out=flat(ob[q % 2][:]), in0=flat(ea[:]), scalar=-1.0,
                                                 in1=flat(ob[q % 2][:]), op0=ALU.add, op1=ALU.add).then_inc(l_out, 1)
                    if step == MF + 2 and has(it, k):
                        residual(it, k, 0)
                    if step == MF + 3 and has(it, k + 2):
                        dve.wait_ge(exps, stage(it, k + 2, 1, 1))
                        dve.tensor_tensor(flat(e1[:]), flat(e1[:]), flat(e2[:]), ALU.max).then_inc(probs, 1)
                    if step == MF + 3 and l1 and phase == 1:
                        dve.wait_ge(l_exps, group(it, q, 1, 1))
                        dve.tensor_tensor(flat(le1[:]), flat(le1[:]), flat(le2[:]), ALU.max).then_inc(l_probs, 1)

            walk(dve, window)

        @block.gpsimd
        def _(pool):
            pool.memset(ident[:], 0.0).then_inc(zeroed, 1)
            pool.wait_ge(zeroed, 1)
            pool.affine_select(out=ident[:], in_=ident[:], compare_op=ALU.not_equal, fill=1.0, base=0,
                               pattern=[[-1, P]], channel_multiplier=1).then_inc(made, 1)
            pool.memset(onescol[:], 1.0).then_inc(made, 1)
            pool.memset(mhalf[:], -0.5).then_inc(made, 1)
            pool.wait_ge(consts_in, 16 * CONSTS)
            apart(pool)
            pool.tensor_scalar(g1s[:], g1col[:], WSCALE, None, ALU.mult).then_inc(made, 1)
            pool.tensor_tensor(rows[:, :, 1, :], rows[:, :, 1, :], b2row, ALU.add).then_inc(made, 1)
            pool.wait_ge(made, 5)

            def inverse_std(mv, ln, s, at):
                apart(pool)
                pool.tensor_scalar(ln[:, 0, :], mv[:, :, 1], EPS, None, ALU.add).then_inc(s, 1)
                pool.wait_ge(s, at(1))
                pool.tensor_tensor(ln[:, 1, :], ln[:, 0, :], mhalf[:], ALU.pow).then_inc(s, 1)
                pool.wait_ge(s, at(2))
                pool.tensor_tensor(ln[:, 2, :], mv[:, :, 0], ln[:, 1, :], ALU.mult).then_inc(s, 1)
                pool.wait_ge(s, at(3))
                apart(pool)
                pool.tensor_scalar(ln[:, 3, :], ln[:, 2, :], -1.0, None, ALU.mult).then_inc(s, 1)

            def shifts(t, c, s, at):
                pool.tensor_tensor(t[:, 1, :], t[:, 0, :], c, ALU.add).then_inc(s, 1)
                pool.wait_ge(s, at(1))
                apart(pool)
                pool.tensor_scalar(t[:, 2, :], t[:, 1, :], SLOPE, None, ALU.mult).then_inc(s, 1)
                pool.tensor_scalar(t[:, 1, :], t[:, 1, :], 0.0, 1.0 - SLOPE, ALU.max, ALU.mult).then_inc(s, 1)
                pool.tensor_scalar(t[:, 5, :], c, SLOPE, None, ALU.mult).then_inc(s, 1)
                pool.wait_ge(s, at(4))
                pool.tensor_tensor(t[:, 3, :], t[:, 1, :], t[:, 2, :], ALU.add).then_inc(s, 1)
                pool.wait_ge(s, at(5))
                pool.tensor_tensor(t[:, 4, :], c, t[:, 3, :], ALU.subtract).then_inc(s, 1)
                pool.tensor_tensor(t[:, 6, :], t[:, 5, :], t[:, 3, :], ALU.subtract).then_inc(s, 1)

            def window(it, k):
                q, phase = l1_of(k)
                l1 = has_group(it, q)
                if has(it, k - 1):
                    pool.wait_ge(ln2_stats, stage(it, k - 1, 3, 3))
                    inverse_std(mv2, ln2, ln2_small, lambda j: stage(it, k - 1, 4, j))
                if has(it, k + 3) and layer(k + 3) == 0:
                    g = (k + 3) // PER * SLOTS + (k + 3) % PER
                    pool.wait_ge(p_stats, group(it, g, 2, 2))
                    if not isinstance(it, int) or it * SLOTS + g >= 1:
                        pool.wait_ge(relu_ok, group(it, g, 1, 0))
                    inverse_std(mv0, ln0, p_small, lambda j: group(it, g, 4, j))
                if has(it, k - 1):
                    l, s = layer(k - 1), (k - 1) % SLOTS
                    last_layer = l == L - 1
                    pool.wait_ge(n2_ok, stage(it, k - 1, 1, 1))
                    pool.tensor_tensor(rr[:], rr[:], rows[:, l, 2:3, :].broadcast_to((P, GB, D)),
                                       ALU.mult).then_inc(x_ok, 1)
                    pool.wait_ge(x_ok, stage(it, k - 1, 2, 1))
                    dst = rr if last_layer else xs[s]
                    pool.tensor_tensor(dst[:], rr[:], rows[:, l, 3:4, :].broadcast_to((P, GB, D)),
                                       ALU.add).then_inc(x_ok, 1)
                    if last_layer:
                        g = (k - 1) // PER * SLOTS + s
                        pool.wait_ge(x_ok, stage(it, k - 1, 2, 2))
                        pool.wait_ge(res_in[s], (it + (k - 1) // PER) * 16 + 16)
                        pool.tensor_tensor(x1[s][:], x1[s][:], rr[:], ALU.add).then_inc(x1_ok, 1)
                if l1 and phase == 0:
                    pool.wait_ge(l_stats, group(it, q, 2, 2))
                    inverse_std(mv3, ln3, l_small, lambda j: group(it, q, 4, j))
                if has(it, k + 1):
                    pool.wait_ge(y_ok, stage(it, k + 1, 5, 5))
                    inverse_std(mv1, ln1, ln1_small, lambda j: stage(it, k + 1, 4, j))
                if has(it, k + 3) and layer(k + 3) == 0:
                    g = (k + 3) // PER * SLOTS + (k + 3) % PER
                    pool.wait_ge(adj_in, group(it, g, 16, 16))
                    apart(pool)
                    pool.tensor_copy(adjt[:], adjin[:]).then_inc(mask0_ok, 1)
                    pool.wait_ge(mask0_ok, group(it, g, 3, 1))
                    pool.tensor_tensor(adjt[:], adjt[:], ident[:].rearrange("p (a j) -> p a j", a=1)
                                       .broadcast_to((P, GB, P)), ALU.add).then_inc(mask0_ok, 1)
                    pool.wait_ge(mask0_ok, group(it, g, 3, 2))
                    apart(pool)
                    pool.tensor_scalar(mask0[g % SLOTS][:], adjt[:], 0.0, -BIG, ALU.is_le, ALU.mult).then_inc(mask0_ok, 1)
                if l1 and phase == 0:
                    pool.wait_ge(adj1_in, group(it, q, 16, 16))
                    apart(pool)
                    pool.tensor_scalar(mask1[:], adj1[:], 0.0, -BIG, ALU.is_equal, ALU.mult).then_inc(mask1_ok, 1)
                if l1 and phase == 1:
                    pool.wait_ge(l_masked, group(it, q, 1, 1))
                    shifts(lsm, lscol[:, GB:2 * GB], l_soft, lambda j: group(it, q, 7, j))
                if l1 and phase == 2:
                    pool.wait_ge(l_hp, group(it, q, 3, 3))
                    apart(pool)
                    pool.tensor_scalar(ea[:], hp[:], 0.0, None, ALU.min).then_inc(l_min, 1)
                if has(it, k + 1):
                    l, h = layer(k + 1), (k + 1) % 2
                    pool.wait_ge(n_ok, stage(it, k + 1, 1, 1))
                    pool.tensor_tensor(rb[h][:], yb[:], rows[:, l, 0:1, :].broadcast_to((P, GB, D)),
                                       ALU.mult).then_inc(rb_ok, 1)
                    pool.wait_ge(rb_ok, stage(it, k + 1, 2, 1))
                    pool.tensor_tensor(rb[h][:], rb[h][:], rows[:, l, 1:2, :].broadcast_to((P, GB, D)),
                                       ALU.add).then_inc(rb_ok, 1)
                if has(it, k + 2):
                    s = (k + 2) % SLOTS
                    pool.wait_ge(masked, stage(it, k + 2, 1, 1))
                    apart(pool)
                    pool.tensor_scalar(sm[:, 7, :], scol[s][:, GB:2 * GB], abias[:, layer(k + 2), 0:1], None,
                                       ALU.add).then_inc(soft_small, 1)
                    pool.wait_ge(soft_small, stage(it, k + 2, 8, 1))
                    shifts(sm, sm[:, 7, :], soft_small, lambda j: stage(it, k + 2, 8, 1 + j))

            walk(pool, window)


_INS = ['x', 'adj', 'L0_gnn_attn_w', 'L0_gnn_attn_b', 'L0_gnn_W1', 'L0_gnn_b1', 'L0_gnn_W2', 'L0_gnn_b2',
        'L0_gnn_g1', 'L0_gnn_beta1', 'L0_gnn_g2', 'L0_gnn_beta2', 'L1_gnn_W', 'L1_gnn_a1', 'L1_gnn_a2']
_OUTS = [((128, 128, 256), 'float32')]


def kernel(**inputs):
    import numpy as _np
    import concourse.bacc as _bacc
    from concourse import mybir as _mybir
    from concourse.bass_utils import run_bass_kernel_spmd as _run

    nc = _bacc.Bacc("TRN2", target_bir_lowering=False, num_devices=1)
    arrays, args = {}, []
    for name in _INS:
        a = _np.ascontiguousarray(inputs[name])
        arrays[f"in_{name}_dram"] = a
        args.append(nc.dram_tensor(f"in_{name}_dram", a.shape, _mybir.dt.from_np(a.dtype), kind="ExternalInput").ap())
    for i, (shape, dtype) in enumerate(_OUTS):
        dt = _mybir.dt.from_np(_np.dtype(dtype))
        args.append(nc.dram_tensor(f"out_{i}_dram", shape, dt, kind="ExternalOutput").ap())
    graph_networks_kernel(nc, *args)
    r = _run(nc, [arrays], core_ids=[0])
    got = tuple(r.results[0][f"out_{i}_dram"] for i in range(len(_OUTS)))
    return got[0]
```

```python
from contextlib import ExitStack

import concourse.bass as bass
from concourse import mybir

ALU = mybir.AluOpType
ACT = mybir.ActivationFunctionType
AX_X = mybir.AxisListType.X
F32 = mybir.dt.float32
F16 = mybir.dt.float16
BF16 = mybir.dt.bfloat16
I32 = mybir.dt.int32

P = 128
EPS = 1e-5
SLOPE = 0.2
BIG = float(2.0 ** 100)
WSCALE = 64.0
LEAST = -3.0e38

GB = 4
SLOTS = 4
FIRST = -3


def graph_networks_kernel(nc, x, adj, attn_w, attn_b, W1, b1, W2, b2, g1, beta1, g2, beta2,
                          L1_W, L1_a1, L1_a2, out):
    B, NODES, D = x.shape
    L = attn_w.shape[0]
    F = W1.shape[2]
    assert NODES == P and D == 2 * P and F % P == 0 and B % (GB * SLOTS) == 0
    KD = D // P
    MF = F // P
    T = GB * P
    PER = L * SLOTS
    ITERS = B // (GB * SLOTS)
    STAGES = ITERS * PER
    GROUPS = ITERS * SLOTS
    LAG1 = PER - 2
    assert L == 3 and ITERS >= 3
    LAST = 3 * GROUPS + LAG1

    def stage(it, k, per, upto):
        return it * (PER * per) + (k * per + upto)

    def group(it, s, per, upto):
        return it * (SLOTS * per) + (s * per + upto)

    def has(it, k):
        return not isinstance(it, int) or 0 <= it * PER + k < STAGES

    def has_group(it, s):
        return not isinstance(it, int) or 0 <= it * SLOTS + s < GROUPS

    def layer(k):
        return (k % PER) // SLOTS

    def l1_of(k):
        return (k - LAG1) // 3, (k - LAG1) % 3

    def apart(eng):
        eng.sem_inc(carrier, 1)

    def walk(eng, window):
        for k in range(FIRST, PER):
            window(0, k)
        with eng.Fori(1, ITERS - 1) as it:
            for k in range(PER):
                window(it, k)
        for k in range(LAST + 1 - (ITERS - 1) * PER):
            window(ITERS - 1, k)

    def prepared(it, k):
        return [k - FIRST] if isinstance(it, int) and it == 0 and k < FIRST + L else []

    with ExitStack() as ctx:
        def sb(name, shape, dt=F32):
            return ctx.enter_context(nc.sbuf_tensor(name, [P] + shape, dt))

        def bank(name):
            return ctx.enter_context(nc.psum_tensor(name, [P, T], F32))

        def sem(name):
            return ctx.enter_context(nc.semaphore(name))

        psH = [bank(f"psH{i}") for i in range(2)]
        psY = [bank(f"psY{i}") for i in range(2)]
        psG = [bank(f"psG{i}") for i in range(2)]
        psT0 = bank("psT0")
        psT1 = bank("psT1")

        w1h = sb("w1h", [L, KD, F], F16)
        w1l = sb("w1l", [L, KD, F], F16)
        w2h = sb("w2h", [L, MF, D], F16)
        w2l = sb("w2l", [L, MF, D], F16)
        b1col = sb("b1col", [L, MF])
        b1raw = sb("b1raw", [L, MF])
        g1col = sb("g1col", [L, KD])
        g1s = sb("g1s", [L, KD])
        be1col = sb("be1col", [L, KD])
        rows = sb("rows", [L, 6, D])
        abias = sb("abias", [L, 1])
        l1w = sb("l1w", [KD, D])
        l1a = sb("l1a", [KD, 2])
        uu = sb("uu", [2, D])
        ident = sb("ident", [P])
        mhalf = sb("mhalf", [GB])

        xin = sb("xin", [GB, D])
        adjin = sb("adjin", [GB, P], I32)
        adjt = sb("adjt", [GB, P])
        xs = [sb(f"xs{i}", [GB, D]) for i in range(SLOTS)]
        x1 = [sb(f"x1_{i}", [GB, D]) for i in range(SLOTS)]
        mask0 = [sb(f"mask0_{i}", [GB, P], BF16) for i in range(SLOTS)]
        scol = [sb(f"scol{i}", [2 * GB]) for i in range(SLOTS)]
        junk = sb("junk", [2 * GB, D], BF16)

        vv = sb("vv", [GB, P])
        e1 = sb("e1", [GB, P])
        e2 = sb("e2", [GB, P])
        pts = sb("pts", [GB, P])
        sm = sb("sm", [8, GB])
        rsum = sb("rsum", [GB])
        rinv = sb("rinv", [GB])
        yb = sb("yb", [GB, D])
        st1 = sb("st1", [GB, 6])
        mv1 = sb("mv1", [GB, 2])
        ln1 = sb("ln1", [4, GB])
        rb = [sb(f"rb{i}", [GB, D]) for i in range(2)]
        hth = [sb(f"hth{i}", [KD, T], F16) for i in range(2)]
        htl = [sb(f"htl{i}", [KD, T], F16) for i in range(2)]

        gf = [sb(f"gf{i}", [T]) for i in range(3)]
        ghi = sb("ghi", [MF, T], F16)
        glo = sb("glo", [MF, T], F16)
        rr = sb("rr", [GB, D])
        st2 = sb("st2", [GB, 6])
        mv2 = sb("mv2", [GB, 2])
        ln2 = sb("ln2", [4, GB])

        st0 = sb("st0", [GB, 6])
        mv0 = sb("mv0", [GB, 2])
        ln0 = sb("ln0", [4, GB])

        adj1 = sb("adj1", [GB, P], I32)
        mask1 = sb("mask1", [GB, P], BF16)
        st3 = sb("st3", [GB, 6])
        mv3 = sb("mv3", [GB, 2])
        ln3 = sb("ln3", [4, GB])
        hl = sb("hl", [GB, D])
        lscol = sb("lscol", [2 * GB])
        lv = sb("lv", [GB, P])
        le1 = sb("le1", [GB, P])
        le2 = sb("le2", [GB, P])
        lpts = sb("lpts", [GB, P])
        lsm = sb("lsm", [8, GB])
        lrsum = sb("lrsum", [GB])
        lrinv = sb("lrinv", [GB])
        hp = sb("hp", [GB, D])
        ea = sb("ea", [GB, D])
        b2row = ea[:, 0:L, :]
        ob = [sb(f"ob{i}", [GB, D]) for i in range(2)]

        stage_w = [g[:].rearrange("p a b -> p (a b)").bitcast(F32) for g in (ghi, glo)]

        consts_in = sem("consts_in")
        stage_in = [sem(f"stage_in{i}") for i in range(2)]
        x_in = sem("x_in")
        adj_in = sem("adj_in")
        res_in = [sem(f"res_in{i}") for i in range(SLOTS)]
        adj1_in = sem("adj1_in")
        out_st = [sem(f"out_st{i}") for i in range(2)]

        made = sem("made")
        zeroed = sem("zeroed")
        carrier = sem("carrier")
        b1_ps = sem("b1_ps")
        b1_ok = sem("b1_ok")
        uu_ps = sem("uu_ps")
        uu_ok = sem("uu_ok")
        scaled = sem("scaled")
        w_hi = sem("w_hi")
        w_ok = sem("w_ok")

        p_stats = sem("p_stats")
        p_small = sem("p_small")
        relu_ok = sem("relu_ok")
        mask0_ok = sem("mask0_ok")
        score_cols = sem("score_cols")
        sj_ps = sem("sj_ps")
        masked = sem("masked")
        soft_small = sem("soft_small")
        exps = sem("exps")
        probs = sem("probs")
        pt_ps = sem("pt_ps")
        pt_ok = sem("pt_ok")
        agg_ps = sem("agg_ps")
        y_ok = sem("y_ok")
        ln1_small = sem("ln1_small")
        n_ok = sem("n_ok")
        nt_ps = sem("nt_ps")
        h_hi = sem("h_hi")
        h_lo = sem("h_lo")
        rb_ok = sem("rb_ok")
        ffn1_ps = sem("ffn1_ps")
        gelu_ok = sem("gelu_ok")
        g_hi = sem("g_hi")
        g_ok = sem("g_ok")
        ffn2_ps = sem("ffn2_ps")
        r_ok = sem("r_ok")
        ln2_stats = sem("ln2_stats")
        ln2_small = sem("ln2_small")
        n2_ok = sem("n2_ok")
        x_ok = sem("x_ok")
        x1_ok = sem("x1_ok")

        l_stats = sem("l_stats")
        l_small = sem("l_small")
        l_relu = sem("l_relu")
        mask1_ok = sem("mask1_ok")
        l_cols = sem("l_cols")
        l_sj = sem("l_sj")
        l_masked = sem("l_masked")
        l_soft = sem("l_soft")
        l_exps = sem("l_exps")
        l_probs = sem("l_probs")
        l_pt = sem("l_pt")
        l_pt_ok = sem("l_pt_ok")
        l_agg = sem("l_agg")
        l_recip = sem("l_recip")
        l_hp = sem("l_hp")
        l_min = sem("l_min")
        l_ea = sem("l_ea")
        l_out = sem("l_out")

        x_dram = x.rearrange("(g b) n d -> n g b d", b=GB)
        out_dram = out.rearrange("(g b) n d -> n g b d", b=GB)
        adj_dram = adj.rearrange("(g b) i j -> i g b j", b=GB)
        CONSTS = 3 * L + 7 + 3

        def grp(dram, it, s):
            return dram[:, bass.ds(it * SLOTS + s, 1), :, :].rearrange("n g b d -> n (g b) d")

        def flat(t):
            return t.rearrange("p b d -> p (b d)")

        block = ctx.enter_context(nc.Block())

        @block.sync
        def _(sp):
            def piece(n):
                if n >= 2:
                    sp.wait_ge(w_ok, n - 1)
                src = (W2 if n % 2 == 0 else W1)[n // 2].rearrange("(k p) f -> p k f", p=P)
                dst = stage_w[n % 2].rearrange("p (k f) -> p k f", k=src.shape[1])
                sp.dma_start(dst, src).then_inc(stage_in[n % 2], 16)

            def load_nodes(it, s):
                if not isinstance(it, int) or it * SLOTS + s >= 1:
                    sp.wait_ge(relu_ok, group(it, s, 1, 0))
                apart(sp)
                sp.dma_start(xin[:], grp(x_dram, it, s)).then_inc(x_in, 16)

            def load_edges(it, s):
                if not isinstance(it, int) or it * SLOTS + s >= 1:
                    sp.wait_ge(mask0_ok, group(it, s - 1, 3, 1))
                apart(sp)
                sp.dma_start(adjin[:], grp(adj_dram, it, s)).then_inc(adj_in, 16)

            load_nodes(0, 0)
            load_edges(0, 0)
            piece(1)
            for src, dst in ((b1, b1raw), (g1, g1col), (beta1, be1col)):
                for l in range(L):
                    with nc.allow_non_contiguous_dma(reason="a small constant"):
                        sp.dma_start(dst[:, l, :], src[l].rearrange("(k p) -> p k", p=P)).then_inc(consts_in, 16)
            for dst, src in ((rows[:, :, 0], g1), (rows[:, :, 1], beta1), (b2row, b2), (rows[:, :, 2], g2),
                             (rows[:, :, 3], beta2), (rows[:, :, 4:6].rearrange("p l a d -> p l (a d)"), attn_w)):
                sp.dma_start(dst, src.rearrange("(a l) d -> a l d", a=1).broadcast_to((P, L, src.shape[1]))
                             ).then_inc(consts_in, 16)
            with nc.allow_non_contiguous_dma(reason="a small constant"):
                sp.dma_start(abias[:].rearrange("p l a -> p (l a)"), attn_b.rearrange("(a l) -> a l", a=1)
                             .broadcast_to((P, L))).then_inc(consts_in, 16)
            sp.dma_start(l1w[:], L1_W.rearrange("(k p) f -> p k f", p=P)).then_inc(consts_in, 16)
            with nc.allow_non_contiguous_dma(reason="a small constant"):
                for i, a in enumerate((L1_a1, L1_a2)):
                    sp.dma_start(l1a[:, :, i:i + 1], a.rearrange("(k p) o -> p k o", p=P)).then_inc(consts_in, 16)
            piece(0)

            def window(it, k):
                if has(it, k + 4) and layer(k + 4) == 0:
                    load_nodes(it, (k + 4) // PER * SLOTS + (k + 4) % PER)
                if has(it, k) and layer(k) == 2:
                    s = k % SLOTS
                    if not isinstance(it, int) or it >= 1:
                        sp.wait_ge(l_out, group(it, s - SLOTS, 2, 2))
                    apart(sp)
                    sp.dma_start(x1[s][:], grp(x_dram, it, s)).then_inc(res_in[s], 16)
                q, phase = l1_of(k + 2)
                if phase == 0 and has_group(it, q):
                    if not isinstance(it, int) or it * SLOTS + q >= 1:
                        sp.wait_ge(mask1_ok, group(it, q, 1, 0))
                    apart(sp)
                    sp.dma_start(adj1[:], grp(adj_dram, it, q)).then_inc(adj1_in, 16)
                q, phase = l1_of(k)
                if phase == 0 and has_group(it, q - 1):
                    sp.wait_ge(l_out, group(it, q - 1, 2, 2))
                    apart(sp)
                    sp.dma_start(grp(out_dram, it, q - 1), ob[(q - 1) % 2][:]).then_inc(out_st[(q - 1) % 2], 16)
                if has(it, k + 4) and layer(k + 4) == 0:
                    load_edges(it, (k + 4) // PER * SLOTS + (k + 4) % PER)
                for l in prepared(it, k):
                    if l + 1 < L:
                        piece(2 * l + 2)
                        piece(2 * l + 3)

            walk(sp, window)
            for o in out_st:
                sp.wait_ge(o, 16 * (GROUPS // 2))

        @block.tensor
        def _(pe):
            def hidden_bias(l):
                pe.wait_ge(stage_in[1], 16 * (l + 1))
                if l == 0:
                    pe.wait_ge(consts_in, 16 * CONSTS)
                w = stage_w[1].rearrange("p (k f) -> p k f", k=KD)
                if l >= 1:
                    pe.wait_ge(b1_ok, l)
                for m in range(MF):
                    for c in range(KD):
                        last = pe.matmul(psH[0][:, m:m + 1], w[:, c, m * P:(m + 1) * P],
                                         be1col[:, l, c:c + 1], start=(c == 0), stop=(c == KD - 1))
                last.then_inc(b1_ps, 1)

            def folded_scores():
                for i in range(2):
                    for c in range(KD):
                        last = pe.matmul(psH[1][:, i * D:(i + 1) * D],
                                         l1a[:, c, i:i + 1].broadcast_to((P, P)), l1w[:, c, :],
                                         start=(c == 0), stop=(c == KD - 1))
                last.then_inc(uu_ps, 1)

            def score_rows(cols, done):
                for b in range(GB):
                    last = pe.matmul(psT0[:, b * P:(b + 1) * P], cols[:, b:b + 1].broadcast_to((P, P)),
                                     ident[:], start=True, stop=True)
                last.then_inc(done, 1)

            def turn_probs(src, done):
                for b in range(GB):
                    last = pe.transpose(psT1[:, b * P:(b + 1) * P], src[:, b, :], ident[:])
                last.then_inc(done, 1)

            def aggregate(pt, vals, done):
                for b in range(GB):
                    last = pe.matmul(psG[b // 2][:, b % 2 * D:(b % 2 + 1) * D], pt[:, b, :], vals[:, b, :],
                                     start=True, stop=True)
                    if b % 2:
                        last.then_inc(done, 1)

            def ffn1(it, k, m):
                l, h = layer(k), k % 2
                if m == 0:
                    pe.wait_ge(h_lo, stage(it, k, 2, 2))
                    if isinstance(it, int) and it == 0 and k % SLOTS == 0:
                        pe.wait_ge(w_ok, 2 * l + 2)
                if m >= 2 or has(it, k - 1):
                    pe.wait_ge(gelu_ok, stage(it, k, MF, m - 1))
                n = 0
                for c in range(KD):
                    for w, t in ((w1h, hth), (w1h, htl), (w1l, hth)):
                        last = pe.matmul(psH[m % 2][:], w[:, l, c, m * P:(m + 1) * P], t[h][:, c, :],
                                         start=(n == 0), stop=(n == 3 * KD - 1))
                        n += 1
                last.then_inc(ffn1_ps, 1)

            def ffn2(it, k, c):
                l = layer(k)
                if c == 0 and has(it, k - 1):
                    pe.wait_ge(r_ok, stage(it, k - 1, 2, 2))
                pe.wait_ge(g_ok, stage(it, k, MF, c + 1))
                for b in range(GB):
                    for n, (g, w) in enumerate(((ghi, w2h), (ghi, w2l), (glo, w2h))):
                        last = pe.matmul(psY[b // 2][:, b % 2 * D:(b % 2 + 1) * D],
                                         g[:, c, b * P:(b + 1) * P], w[:, l, c, :],
                                         start=(c == 0 and n == 0 and b % 2 == 0),
                                         stop=(c == MF - 1 and n == 2), skip_group_check=True)
                    if c == MF - 1 and b % 2:
                        last.then_inc(ffn2_ps, 1)

            pe.wait_ge(made, 1)

            def window(it, k):
                q, phase = l1_of(k)
                l1 = has_group(it, q)
                if isinstance(it, int) and it == 0 and k == 0:
                    pe.wait_ge(b1_ok, L)
                    pe.wait_ge(uu_ok, 1)
                for step in range(MF):
                    if has(it, k):
                        ffn1(it, k, step)
                    if step == 0 and l1 and phase == 1:
                        if has(it, k):
                            pe.wait_ge(h_lo, stage(it, k, 2, 1))
                        pe.wait_ge(l_cols, group(it, q, 2, 1))
                        score_rows(lscol, l_sj)
                    if step == 1 and has(it, k + 1):
                        pe.wait_ge(probs, stage(it, k + 1, 1, 1))
                        turn_probs(e1, pt_ps)
                    if step == 2 and has(it, k + 1):
                        pe.wait_ge(pt_ok, stage(it, k + 1, 1, 1))
                        if phase == 0 and has_group(it, q - 1):
                            pe.wait_ge(l_hp, group(it, q - 1, 2, 2))
                        aggregate(pts, xs[(k + 1) % SLOTS], agg_ps)
                    if step == 3 and has(it, k + 2):
                        if l1 and phase == 1:
                            pe.wait_ge(l_masked, group(it, q, 1, 1))
                        elif has(it, k):
                            pe.wait_ge(h_lo, stage(it, k, 2, 1))
                        pe.wait_ge(score_cols, stage(it, k + 2, 2, 1))
                        score_rows(scol[(k + 2) % SLOTS], sj_ps)
                    if step == 3 and l1 and phase == 2:
                        pe.wait_ge(l_probs, group(it, q, 1, 1))
                        turn_probs(le1, l_pt)
                    if step == 5 and l1 and phase == 2:
                        if has(it, k + 1):
                            pe.wait_ge(y_ok, stage(it, k + 1, 4, 2))
                        pe.wait_ge(l_pt_ok, group(it, q, 1, 1))
                        aggregate(lpts, hl, l_agg)
                    if step == 6 and has(it, k + 1):
                        pe.wait_ge(n_ok, stage(it, k + 1, 1, 1))
                        if has(it, k + 2):
                            pe.wait_ge(masked, stage(it, k + 2, 1, 1))
                        elif l1 and phase == 1:
                            pe.wait_ge(l_masked, group(it, q, 1, 1))
                        if l1 and phase == 2:
                            pe.wait_ge(l_pt_ok, group(it, q, 1, 1))
                        for c, ps in enumerate((psT0, psT1)):
                            for b in range(GB):
                                last = pe.transpose(ps[:, b * P:(b + 1) * P], yb[:, b, c * P:(c + 1) * P], ident[:])
                            last.then_inc(nt_ps, 1)
                    if step < 2 and has(it, k - 1):
                        ffn2(it, k - 1, MF - 2 + step)
                    if step >= 2 and has(it, k):
                        ffn2(it, k, step - 2)

                for l in prepared(it, k):
                    hidden_bias(l)
                    if l == 0:
                        folded_scores()

            walk(pe, window)

        @block.scalar
        def _(act):
            def scale_piece(n):
                l = n // 2
                act.wait_ge(stage_in[n % 2], 16 * (l + 1))
                if n % 2 == 1:
                    if l == 0:
                        act.wait_ge(made, 3)
                    act.wait_ge(b1_ps, l + 1)
                    for c in range(KD):
                        w = stage_w[1][:, c * F:(c + 1) * F]
                        last = act.activation(w, w, ACT.Copy, scale=g1s[:, l, c:c + 1])
                else:
                    last = act.activation(stage_w[0], stage_w[0], ACT.Copy, scale=WSCALE)
                last.then_inc(scaled, 1)

            def norm(dst, src, ln, func):
                for b in range(GB):
                    last = act.activation(dst[:, b, :], src[:, b, :], func,
                                          bias=ln[:, 3, b:b + 1], scale=ln[:, 1, b:b + 1])
                return last

            def two_exps(v, s, ea_, eb_):
                for b in range(GB):
                    act.activation(ea_[:, b, :], v[:, b, :], ACT.Exp, bias=s[:, 4, b:b + 1])
                for b in range(GB):
                    last = act.activation(eb_[:, b, :], v[:, b, :], ACT.Exp, bias=s[:, 6, b:b + 1], scale=SLOPE)
                return last

            def gelu(it, k, m):
                act.wait_ge(ffn1_ps, stage(it, k, MF, m + 1))
                if has(it, k - 1) or m >= 3:
                    act.wait_ge(g_ok, stage(it, k, MF, m - 2))
                n = (k * MF + m) % 3
                act.activation(gf[n][:], psH[m % 2][:], ACT.Gelu, bias=b1col[:, layer(k), m:m + 1],
                               scale=1.0 / WSCALE).then_inc(gelu_ok, 1)

            def window(it, k):
                q, phase = l1_of(k)
                l1 = has_group(it, q)
                if isinstance(it, int) and it == 0 and k == 0:
                    act.wait_ge(b1_ok, L)
                for step in range(MF):
                    if step == 7 and has(it, k + 2):
                        act.wait_ge(soft_small, stage(it, k + 2, 8, 8))
                        two_exps(vv, sm, e1, e2).then_inc(exps, 1)
                    if has(it, k):
                        gelu(it, k, step)
                    if step == 7 and l1 and phase == 2:
                        act.wait_ge(l_min, group(it, q, 1, 1))
                        act.activation(ea[:], ea[:], ACT.Exp).then_inc(l_ea, 1)
                    if step == 1 and has(it, k + 1):
                        act.wait_ge(pt_ps, stage(it, k + 1, 1, 1))
                        act.activation(flat(pts[:]), psT1[:], ACT.Copy).then_inc(pt_ok, 1)
                    if step == 3 and l1 and phase == 0:
                        act.wait_ge(l_small, group(it, q, 4, 4))
                        norm(hl, x1[q % SLOTS], ln3, ACT.Relu).then_inc(l_relu, 1)
                    if step == 2 and has(it, k + 3) and layer(k + 3) == 0:
                        g = (k + 3) // PER * SLOTS + (k + 3) % PER
                        act.wait_ge(p_small, group(it, g, 4, 4))
                        norm(xs[g % SLOTS], xin, ln0, ACT.Relu).then_inc(relu_ok, 1)
                    if step == 3 and l1 and phase == 2:
                        act.wait_ge(l_pt, group(it, q, 1, 1))
                        act.activation(flat(lpts[:]), psT1[:], ACT.Copy).then_inc(l_pt_ok, 1)
                    if step == 3 and has(it, k - 1):
                        act.wait_ge(ln2_small, stage(it, k - 1, 4, 4))
                        norm(rr, rr, ln2, ACT.Identity).then_inc(n2_ok, 1)
                    if step == 2 and l1 and phase == 1:
                        act.wait_ge(l_soft, group(it, q, 7, 7))
                        two_exps(lv, lsm, le1, le2).then_inc(l_exps, 1)
                    if step == 5 and has(it, k + 1):
                        act.wait_ge(ln1_small, stage(it, k + 1, 4, 4))
                        norm(yb, yb, ln1, ACT.Identity).then_inc(n_ok, 1)
                    if step == 6 and has(it, k + 1):
                        for c, ps in enumerate((psT0, psT1)):
                            act.wait_ge(nt_ps, stage(it, k + 1, 2, c + 1))
                            act.activation(hth[(k + 1) % 2][:, c, :], ps[:], ACT.Copy).then_inc(h_hi, 1)

                for l in prepared(it, k):
                    scale_piece(2 * l)
                    scale_piece(2 * l + 1)

            walk(act, window)

        @block.vector
        def _(dve):
            def split_piece(n):
                l = n // 2
                hi, lo = ((w2h, w2l), (w1h, w1l))[n % 2]
                hi, lo = (t[:, l].rearrange("p a b -> p (a b)") for t in (hi, lo))
                dve.wait_ge(scaled, n + 1)
                dve.tensor_copy(hi, stage_w[n % 2]).then_inc(w_hi, 1)
                dve.wait_ge(w_hi, n + 1)
                dve.tensor_tensor(lo, stage_w[n % 2], hi, ALU.subtract).then_inc(w_ok, 1)

            def hidden_bias(l):
                dve.wait_ge(b1_ps, l + 1)
                dve.tensor_tensor(b1col[:, l, :], psH[0][:, 0:MF], b1raw[:, l, :], ALU.add).then_inc(b1_ok, 1)

            def stats(src, st, lo, hi):
                for b in range(lo, hi):
                    last = dve.bn_stats(st[:, b, :], src[:, b, :])
                return last

            def mean_var(st, mv):
                apart(dve)
                for b in range(GB):
                    last = dve.bn_aggr(mv[:, b, :], st[:, b, :])
                return last

            def dot_scores(src, ws, h, cols):
                for b in range(GB):
                    last = dve.tensor_tensor_reduce(junk[:, h * GB + b, :], src[:, b, :], ws[h], 1.0, 0.0,
                                                    ALU.mult, ALU.add, cols[:, h * GB + b:h * GB + b + 1])
                return last

            def mask_rows(mask, v, s):
                apart(dve)
                for b in range(GB):
                    last = dve.tensor_tensor_reduce(v[:, b, :], psT0[:, b * P:(b + 1) * P], mask[:, b, :], 1.0,
                                                    LEAST, ALU.add, ALU.max, s[:, 0, b:b + 1])
                return last

            def gelu_parts(it, k, m):
                n = (k * MF + m) % 3
                dve.wait_ge(gelu_ok, stage(it, k, MF, m + 1))
                dve.tensor_copy(ghi[:, m, :], gf[n][:]).then_inc(g_hi, 1)
                dve.wait_ge(g_hi, stage(it, k, MF, m + 1))
                dve.tensor_tensor(glo[:, m, :], gf[n][:], ghi[:, m, :], ALU.subtract).then_inc(g_ok, 1)

            def residual(it, k):
                dve.wait_ge(rb_ok, stage(it, k, 2, 2))
                if has(it, k - 1):
                    dve.wait_ge(x_ok, stage(it, k - 1, 2, 2))
                    if layer(k - 1) == 2:
                        dve.wait_ge(x1_ok, group(it, (k - 1) // PER * SLOTS + (k - 1) % SLOTS, 1, 1))
                for pr in range(2):
                    dve.wait_ge(ffn2_ps, stage(it, k, 2, pr + 1))
                    dst = flat(rr[:, 2 * pr:2 * pr + 2, :])
                    dve.scalar_tensor_tensor(out=dst, in0=psY[pr][:], scalar=1.0 / WSCALE,
                                             in1=flat(rb[k % 2][:, 2 * pr:2 * pr + 2, :]),
                                             op0=ALU.mult, op1=ALU.add).then_inc(r_ok, 1)

            def residual_stats(it, k):
                for pr in range(2):
                    dve.wait_ge(r_ok, stage(it, k, 2, pr + 1))
                    last = stats(rr, st2, 2 * pr, 2 * pr + 2)
                last.then_inc(ln2_stats, 1)
                dve.wait_ge(ln2_stats, stage(it, k, 2, 1))
                mean_var(st2, mv2).then_inc(ln2_stats, 1)

            def probabilities(ea_, eb_, sums):
                for b in range(GB):
                    last = dve.scalar_tensor_tensor(out=ea_[:, b, :], in0=ea_[:, b, :], scalar=1.0,
                                                    in1=eb_[:, b, :], op0=ALU.mult, op1=ALU.max,
                                                    accum_out=sums[:, b:b + 1])
                return last

            def window(it, k):
                q, phase = l1_of(k)
                l1 = has_group(it, q)
                for step in range(MF):
                    if step == 0 and l1 and phase == 2:
                        dve.wait_ge(l_exps, group(it, q, 1, 1))
                        probabilities(le1, le2, lrsum).then_inc(l_probs, 1)
                    if step == 0 and has(it, k + 3) and layer(k + 3) == 0:
                        g = (k + 3) // PER * SLOTS + (k + 3) % PER
                        dve.wait_ge(x_in, group(it, g, 16, 16))
                        stats(xin, st0, 0, GB).then_inc(p_stats, 1)
                        dve.wait_ge(p_stats, group(it, g, 2, 1))
                        mean_var(st0, mv0).then_inc(p_stats, 1)
                    if step == 1 and l1 and phase == 0:
                        dve.wait_ge(x1_ok, group(it, q, 1, 1))
                        stats(x1[q % SLOTS], st3, 0, GB).then_inc(l_stats, 1)
                        dve.wait_ge(l_stats, group(it, q, 2, 1))
                        mean_var(st3, mv3).then_inc(l_stats, 1)
                    if step == 1 and l1 and phase == 1:
                        dve.wait_ge(l_sj, group(it, q, 1, 1))
                        dve.wait_ge(mask1_ok, group(it, q, 1, 1))
                        mask_rows(mask1, lv, lsm).then_inc(l_masked, 1)
                    if step in (2, 4) and has(it, k + 2):
                        n, h = k + 2, int(step == 4)
                        if h == 0:
                            if layer(n) == 0:
                                dve.wait_ge(relu_ok, group(it, n // PER * SLOTS + n % PER, 1, 1))
                            else:
                                dve.wait_ge(x_ok, stage(it, n - 4, 2, 2))
                            if has(it, n - 1):
                                dve.wait_ge(score_cols, stage(it, n - 1, 2, 2))
                            if has_group(it, q - (phase == 0)):
                                dve.wait_ge(l_cols, group(it, q - (phase == 0), 2, 2))
                        dot_scores(xs[n % SLOTS], (rows[:, layer(n), 5, :], rows[:, layer(n), 4, :]), h,
                                   scol[n % SLOTS]).then_inc(score_cols, 1)
                    if step == 2 and has(it, k - 1):
                        residual_stats(it, k - 1)
                    if step == 3 and has(it, k + 1):
                        s = (k + 1) % SLOTS
                        dve.wait_ge(probs, stage(it, k + 1, 1, 1))
                        dve.reciprocal(rinv[:], rsum[:]).then_inc(y_ok, 1)
                        dve.wait_ge(y_ok, stage(it, k + 1, 4, 1))
                        if has(it, k):
                            dve.wait_ge(rb_ok, stage(it, k, 2, 1))
                        for b in range(GB):
                            if b % 2 == 0:
                                dve.wait_ge(agg_ps, stage(it, k + 1, 2, 1 + b // 2))
                            last = dve.scalar_tensor_tensor(
                                out=yb[:, b, :], in0=psG[b // 2][:, b % 2 * D:(b % 2 + 1) * D],
                                scalar=rinv[:, b:b + 1], in1=xs[s][:, b, :], op0=ALU.mult, op1=ALU.add)
                        last.then_inc(y_ok, 1)
                        dve.wait_ge(y_ok, stage(it, k + 1, 4, 2))
                        stats(yb, st1, 0, GB).then_inc(y_ok, 1)
                        dve.wait_ge(y_ok, stage(it, k + 1, 4, 3))
                        mean_var(st1, mv1).then_inc(y_ok, 1)
                    if step == 4 and has(it, k + 2):
                        dve.wait_ge(sj_ps, stage(it, k + 2, 1, 1))
                        if layer(k + 2) == 0:
                            g = (k + 2) // PER * SLOTS + (k + 2) % PER
                            dve.wait_ge(mask0_ok, group(it, g, 3, 3))
                        mask_rows(mask0[(k + 2) % SLOTS], vv, sm).then_inc(masked, 1)
                    if step in (4, 5) and l1 and phase == 0:
                        h = int(step == 5)
                        if h == 0:
                            if has(it, k + 2):
                                dve.wait_ge(score_cols, stage(it, k + 2, 2, 2))
                            elif has_group(it, q - 1):
                                dve.wait_ge(l_cols, group(it, q - 1, 2, 2))
                            dve.wait_ge(l_relu, group(it, q, 1, 1))
                        dot_scores(hl, (uu[:, 1, :], uu[:, 0, :]), h, lscol).then_inc(l_cols, 1)
                    if step == 5 and l1 and phase == 2:
                        dve.wait_ge(l_probs, group(it, q, 1, 1))
                        dve.reciprocal(lrinv[:], lrsum[:]).then_inc(l_recip, 1)
                        dve.wait_ge(l_recip, group(it, q, 1, 1))
                        for b in range(GB):
                            if b % 2 == 0:
                                dve.wait_ge(l_agg, group(it, q, 2, 1 + b // 2))
                            last = dve.tensor_scalar(hp[:, b, :], psG[b // 2][:, b % 2 * D:(b % 2 + 1) * D],
                                                     lrinv[:, b:b + 1], None, ALU.mult)
                            if b % 2:
                                last.then_inc(l_hp, 1)
                        dve.wait_ge(l_hp, group(it, q, 2, 2))
                        if not isinstance(it, int) or it * SLOTS + q >= 2:
                            dve.wait_ge(out_st[q % 2], it * (16 * SLOTS // 2) + 16 * (q // 2))
                        dve.scalar_tensor_tensor(out=flat(ob[q % 2][:]), in0=flat(hp[:]), scalar=0.0,
                                                 in1=flat(x1[q % SLOTS][:]), op0=ALU.max, op1=ALU.add).then_inc(l_out, 1)
                    if step == 5 and phase == 0 and has_group(it, q - 1):
                        dve.wait_ge(l_out, group(it, q - 1, 2, 1))
                        dve.wait_ge(l_ea, group(it, q - 1, 1, 1))
                        o = flat(ob[(q - 1) % 2][:])
                        dve.scalar_tensor_tensor(out=o, in0=flat(ea[:]), scalar=-1.0,
                                                 in1=o, op0=ALU.add, op1=ALU.add).then_inc(l_out, 1)
                    if step == 7 and has(it, k + 1):
                        for c, ps in enumerate((psT0, psT1)):
                            dve.wait_ge(h_hi, stage(it, k + 1, 2, c + 1))
                            dve.tensor_tensor(htl[(k + 1) % 2][:, c, :], ps[:], hth[(k + 1) % 2][:, c, :],
                                              ALU.subtract).then_inc(h_lo, 1)
                    if step == 7 and has(it, k + 2):
                        dve.wait_ge(exps, stage(it, k + 2, 1, 1))
                        probabilities(e1, e2, rsum).then_inc(probs, 1)
                    if step == 1 and has(it, k - 1):
                        residual(it, k - 1)
                    if has(it, k):
                        gelu_parts(it, k, step)

                for l in prepared(it, k):
                    split_piece(2 * l)
                    if l == 0:
                        dve.wait_ge(consts_in, 16 * CONSTS)
                    hidden_bias(l)
                    if l == 0:
                        dve.wait_ge(uu_ps, 1)
                        dve.tensor_copy(uu[:].rearrange("p a d -> p (a d)"), psH[1][:]).then_inc(uu_ok, 1)
                    split_piece(2 * l + 1)

            walk(dve, window)

        @block.gpsimd
        def _(pool):
            pool.memset(ident[:], 0.0).then_inc(zeroed, 1)
            pool.wait_ge(zeroed, 1)
            pool.affine_select(out=ident[:], in_=ident[:], compare_op=ALU.not_equal, fill=1.0, base=0,
                               pattern=[[-1, P]], channel_multiplier=1).then_inc(made, 1)
            pool.memset(mhalf[:], -0.5).then_inc(made, 1)
            pool.wait_ge(consts_in, 16 * CONSTS)
            apart(pool)
            pool.tensor_scalar(g1s[:], g1col[:], WSCALE, None, ALU.mult).then_inc(made, 1)
            pool.tensor_tensor(rows[:, :, 1, :], rows[:, :, 1, :], b2row, ALU.add).then_inc(made, 1)
            pool.wait_ge(made, 4)

            def inverse_std(mv, ln, s, at):
                apart(pool)
                pool.tensor_scalar(ln[:, 0, :], mv[:, :, 1], EPS, None, ALU.add).then_inc(s, 1)
                pool.wait_ge(s, at(1))
                pool.tensor_tensor(ln[:, 1, :], ln[:, 0, :], mhalf[:], ALU.pow).then_inc(s, 1)
                pool.wait_ge(s, at(2))
                pool.tensor_tensor(ln[:, 2, :], mv[:, :, 0], ln[:, 1, :], ALU.mult).then_inc(s, 1)
                pool.wait_ge(s, at(3))
                apart(pool)
                pool.tensor_scalar(ln[:, 3, :], ln[:, 2, :], -1.0, None, ALU.mult).then_inc(s, 1)

            def shifts(t, c, s, at):
                pool.tensor_tensor(t[:, 1, :], t[:, 0, :], c, ALU.add).then_inc(s, 1)
                pool.wait_ge(s, at(1))
                apart(pool)
                pool.tensor_scalar(t[:, 2, :], t[:, 1, :], SLOPE, None, ALU.mult).then_inc(s, 1)
                pool.tensor_scalar(t[:, 1, :], t[:, 1, :], 0.0, 1.0 - SLOPE, ALU.max, ALU.mult).then_inc(s, 1)
                pool.tensor_scalar(t[:, 5, :], c, SLOPE, None, ALU.mult).then_inc(s, 1)
                pool.wait_ge(s, at(4))
                pool.tensor_tensor(t[:, 3, :], t[:, 1, :], t[:, 2, :], ALU.add).then_inc(s, 1)
                pool.wait_ge(s, at(5))
                pool.tensor_tensor(t[:, 4, :], c, t[:, 3, :], ALU.subtract).then_inc(s, 1)
                pool.tensor_tensor(t[:, 6, :], t[:, 5, :], t[:, 3, :], ALU.subtract).then_inc(s, 1)

            def window(it, k):
                q, phase = l1_of(k)
                l1 = has_group(it, q)
                if has(it, k + 3) and layer(k + 3) == 0:
                    g = (k + 3) // PER * SLOTS + (k + 3) % PER
                    pool.wait_ge(p_stats, group(it, g, 2, 2))
                    if not isinstance(it, int) or it * SLOTS + g >= 1:
                        pool.wait_ge(relu_ok, group(it, g, 1, 0))
                    inverse_std(mv0, ln0, p_small, lambda j: group(it, g, 4, j))
                if l1 and phase == 0:
                    pool.wait_ge(l_stats, group(it, q, 2, 2))
                    inverse_std(mv3, ln3, l_small, lambda j: group(it, q, 4, j))
                if l1 and phase == 1:
                    pool.wait_ge(l_masked, group(it, q, 1, 1))
                    shifts(lsm, lscol[:, GB:2 * GB], l_soft, lambda j: group(it, q, 7, j))
                if has(it, k - 1):
                    pool.wait_ge(ln2_stats, stage(it, k - 1, 2, 2))
                    inverse_std(mv2, ln2, ln2_small, lambda j: stage(it, k - 1, 4, j))
                if has(it, k + 2) and layer(k + 2) == 0:
                    g = (k + 2) // PER * SLOTS + (k + 2) % PER
                    pool.wait_ge(mask0_ok, group(it, g, 3, 2))
                    apart(pool)
                    pool.tensor_scalar(mask0[g % SLOTS][:], adjt[:], 0.0, -BIG, ALU.is_le, ALU.mult).then_inc(mask0_ok, 1)
                if l1 and phase == 0:
                    pool.wait_ge(adj1_in, group(it, q, 16, 16))
                    apart(pool)
                    pool.tensor_scalar(mask1[:], adj1[:], 0.0, -BIG, ALU.is_equal, ALU.mult).then_inc(mask1_ok, 1)
                if has(it, k + 1):
                    pool.wait_ge(y_ok, stage(it, k + 1, 4, 4))
                    inverse_std(mv1, ln1, ln1_small, lambda j: stage(it, k + 1, 4, j))
                if has(it, k + 2):
                    s = (k + 2) % SLOTS
                    pool.wait_ge(score_cols, stage(it, k + 2, 2, 2))
                    pool.wait_ge(masked, stage(it, k + 2, 1, 1))
                    apart(pool)
                    pool.tensor_scalar(sm[:, 7, :], scol[s][:, GB:2 * GB], abias[:, layer(k + 2), 0:1], None,
                                       ALU.add).then_inc(soft_small, 1)
                    pool.wait_ge(soft_small, stage(it, k + 2, 8, 1))
                    shifts(sm, sm[:, 7, :], soft_small, lambda j: stage(it, k + 2, 8, 1 + j))
                if has(it, k - 1):
                    l, s = layer(k - 1), (k - 1) % SLOTS
                    last_layer = l == L - 1
                    pool.wait_ge(n2_ok, stage(it, k - 1, 1, 1))
                    pool.tensor_tensor(rr[:], rr[:], rows[:, l, 2:3, :].broadcast_to((P, GB, D)),
                                       ALU.mult).then_inc(x_ok, 1)
                    pool.wait_ge(x_ok, stage(it, k - 1, 2, 1))
                    dst = rr if last_layer else xs[s]
                    pool.tensor_tensor(dst[:], rr[:], rows[:, l, 3:4, :].broadcast_to((P, GB, D)),
                                       ALU.add).then_inc(x_ok, 1)
                    if last_layer:
                        g = (k - 1) // PER * SLOTS + s
                        pool.wait_ge(x_ok, stage(it, k - 1, 2, 2))
                        pool.wait_ge(res_in[s], (it + (k - 1) // PER) * 16 + 16)
                        pool.tensor_tensor(x1[s][:], x1[s][:], rr[:], ALU.add).then_inc(x1_ok, 1)
                if l1 and phase == 2:
                    pool.wait_ge(l_hp, group(it, q, 2, 2))
                    apart(pool)
                    pool.tensor_scalar(ea[:], hp[:], 0.0, None, ALU.min).then_inc(l_min, 1)
                if has(it, k + 1):
                    l, h = layer(k + 1), (k + 1) % 2
                    pool.wait_ge(n_ok, stage(it, k + 1, 1, 1))
                    pool.tensor_tensor(rb[h][:], yb[:], rows[:, l, 0:1, :].broadcast_to((P, GB, D)),
                                       ALU.mult).then_inc(rb_ok, 1)
                    pool.wait_ge(rb_ok, stage(it, k + 1, 2, 1))
                    pool.tensor_tensor(rb[h][:], rb[h][:], rows[:, l, 1:2, :].broadcast_to((P, GB, D)),
                                       ALU.add).then_inc(rb_ok, 1)
                if has(it, k + 3) and layer(k + 3) == 0:
                    g = (k + 3) // PER * SLOTS + (k + 3) % PER
                    pool.wait_ge(adj_in, group(it, g, 16, 16))
                    apart(pool)
                    pool.tensor_copy(adjt[:], adjin[:]).then_inc(mask0_ok, 1)
                    pool.wait_ge(mask0_ok, group(it, g, 3, 1))
                    pool.tensor_tensor(adjt[:], adjt[:], ident[:].rearrange("p (a j) -> p a j", a=1)
                                       .broadcast_to((P, GB, P)), ALU.add).then_inc(mask0_ok, 1)

            walk(pool, window)


_INS = ['x', 'adj', 'L0_gnn_attn_w', 'L0_gnn_attn_b', 'L0_gnn_W1', 'L0_gnn_b1', 'L0_gnn_W2', 'L0_gnn_b2',
        'L0_gnn_g1', 'L0_gnn_beta1', 'L0_gnn_g2', 'L0_gnn_beta2', 'L1_gnn_W', 'L1_gnn_a1', 'L1_gnn_a2']
_OUTS = [((128, 128, 256), 'float32')]


def kernel(**inputs):
    import numpy as _np
    import concourse.bacc as _bacc
    from concourse import mybir as _mybir
    from concourse.bass_utils import run_bass_kernel_spmd as _run

    nc = _bacc.Bacc("TRN2", target_bir_lowering=False, num_devices=1)
    arrays, args = {}, []
    for name in _INS:
        a = _np.ascontiguousarray(inputs[name])
        arrays[f"in_{name}_dram"] = a
        args.append(nc.dram_tensor(f"in_{name}_dram", a.shape, _mybir.dt.from_np(a.dtype), kind="ExternalInput").ap())
    for i, (shape, dtype) in enumerate(_OUTS):
        dt = _mybir.dt.from_np(_np.dtype(dtype))
        args.append(nc.dram_tensor(f"out_{i}_dram", shape, dt, kind="ExternalOutput").ap())
    graph_networks_kernel(nc, *args)
    r = _run(nc, [arrays], core_ids=[0])
    got = tuple(r.results[0][f"out_{i}_dram"] for i in range(len(_OUTS)))
    return got[0]
```
